# Optimizing a Trainium2 kernel written in Bass

```python
import numpy as np
import jax
import jax.numpy as jnp

def _softmax(x, axis=-1):
    return jax.nn.softmax(x, axis=axis)

def _gelu(x):
    return jax.nn.gelu(x, approximate=True)

def _silu(x):
    return jax.nn.silu(x)

def _sigmoid(x):
    return jax.nn.sigmoid(x)

def _layernorm(x, axis=-1, eps=1e-05):
    m = jnp.mean(x, axis=axis, keepdims=True)
    v = jnp.var(x, axis=axis, keepdims=True)
    return (x - m) / jnp.sqrt(v + eps)

def _scatter_add(tgt, idx, src, axis=0):
    return tgt.at[idx].add(src)

def _segment_sum(src, seg, n):
    return jax.ops.segment_sum(src, seg, n)
kernel_name = 'mk_gnn_resnorm_d2_gnn_r8_890f8f'

def setup_inputs(seed: int=0):
    np.random.seed(seed)
    _w = jnp.asarray

    def _rec_inputs():
        import jax
        import jax.numpy as jnp
        _gk = jax.random.key(seed)
        x = -0.0005121 + 1.001 * jax.random.normal(jax.random.fold_in(_gk, 1), (12500, 32), jnp.float32)
        src = jax.random.randint(jax.random.fold_in(_gk, 2), (400000,), 0, 12500, jnp.int32)
        dst = jax.random.randint(jax.random.fold_in(_gk, 3), (400000,), 0, 12500, jnp.int32)
        _o = jnp.argsort(dst, stable=True)
        src = src[_o]
        dst = dst[_o]
        edge_attr_2 = jax.random.uniform(jax.random.fold_in(_gk, 12), (400000, 2), jnp.float32, 0.0, 1)
        edge_type_8 = jax.random.randint(jax.random.fold_in(_gk, 14), (400000,), 0, 8, jnp.int32)
        return (x, src, dst, edge_attr_2, edge_type_8)
    x, src, dst, edge_attr_2, edge_type_8 = _rec_inputs()

    def _L0_gnn_setup():
        import jax, jax.numpy as jnp
        import numpy as np
        N_NODES = 12500
        N_EDGES = 400000
        IN_CH = 32
        OUT_CH = 32
        DIM = 2
        KSIZE = 3

        def _basis(pseudo):
            p = jnp.clip(pseudo, 0.0, 1.0)
            grid = jnp.linspace(0.0, 1.0, KSIZE, dtype=p.dtype)
            dist = jnp.abs(p[:, :, None] - grid[None, None, :])
            b = jnp.maximum(1.0 - dist * (KSIZE - 1), 0.0)
            basis = jnp.einsum('ea,eb->eab', b[:, 0], b[:, 1])
            return basis.reshape(p.shape[0], -1)
        key = jax.random.key(seed)
        k1, k2, k3, k4, k5, k6 = jax.random.split(key, 6)
        x = jax.random.normal(k1, (N_NODES, IN_CH), dtype=jnp.float32)
        pseudo = jax.random.uniform(k2, (N_EDGES, DIM), dtype=jnp.float32)
        weight = jax.random.normal(k3, (KSIZE * KSIZE, IN_CH, OUT_CH), dtype=jnp.float32) / np.sqrt(IN_CH)
        root_w = jax.random.normal(k4, (OUT_CH, IN_CH), dtype=jnp.float32) / np.sqrt(IN_CH)
        root_b = jax.random.normal(k5, (OUT_CH,), dtype=jnp.float32) * 0.01
        edge_index = jax.random.randint(k6, (2, N_EDGES), 0, N_NODES, dtype=jnp.int64)
        return {'x': x, 'pseudo': pseudo, 'weight': weight, 'root_w': root_w, 'root_b': root_b, 'edge_index': edge_index}
    _L0_gnn_all = _L0_gnn_setup()
    _L0_gnn_in = {k: v for k, v in _L0_gnn_all.items() if k in ('weight', 'root_w', 'root_b')}
    del _L0_gnn_all

    def _L1_gnn_setup():
        import jax, jax.numpy as jnp
        import numpy as np
        N_NODES = 6250
        N_EDGES = 200000
        D = 32
        NUM_BASES = 4
        NUM_RELATIONS = 8
        key = jax.random.key(seed)
        k = jax.random.split(key, 6)
        x = jax.random.normal(k[0], (N_NODES, D), dtype=jnp.float32)
        W = jax.random.normal(k[1], (NUM_BASES, D, D), dtype=jnp.float32) / np.sqrt(D)
        etw = jax.random.normal(k[2], (NUM_BASES, NUM_RELATIONS), dtype=jnp.float32)
        src = jax.random.randint(k[3], (N_EDGES,), 0, N_NODES, dtype=jnp.int32)
        dst = jax.random.randint(k[4], (N_EDGES,), 0, N_NODES, dtype=jnp.int32)
        edge_type = jax.random.randint(k[5], (N_EDGES,), 0, NUM_RELATIONS, dtype=jnp.int32)
        return {'x': x, 'W': W, 'edge_type_weight': etw, 'src': src, 'dst': dst, 'edge_type': edge_type}
    _L1_gnn_all = _L1_gnn_setup()
    _L1_gnn_in = {k: v for k, v in _L1_gnn_all.items() if k in ('W', 'edge_type_weight')}
    del _L1_gnn_all
    return {'x': x, 'src': src, 'dst': dst, 'edge_attr_2': edge_attr_2, 'edge_type_8': edge_type_8, 'L0_gnn_weight': _L0_gnn_in['weight'], 'L0_gnn_root_w': _L0_gnn_in['root_w'], 'L0_gnn_root_b': _L0_gnn_in['root_b'], 'L1_gnn_W': _L1_gnn_in['W'], 'L1_gnn_edge_type_weight': _L1_gnn_in['edge_type_weight']}

def reference(x, src, dst, edge_attr_2, edge_type_8, L0_gnn_weight, L0_gnn_root_w, L0_gnn_root_b, L1_gnn_W, L1_gnn_edge_type_weight):
    import jax
    import jax.numpy as jnp

    def _L0_gnn_ref(x, pseudo, weight, root_w, root_b, edge_index):
        import jax, jax.numpy as jnp
        import numpy as np
        N_NODES = 12500
        N_EDGES = 400000
        IN_CH = 32
        OUT_CH = 32
        DIM = 2
        KSIZE = 3

        def _basis(pseudo):
            p = jnp.clip(pseudo, 0.0, 1.0)
            grid = jnp.linspace(0.0, 1.0, KSIZE, dtype=p.dtype)
            dist = jnp.abs(p[:, :, None] - grid[None, None, :])
            b = jnp.maximum(1.0 - dist * (KSIZE - 1), 0.0)
            basis = jnp.einsum('ea,eb->eab', b[:, 0], b[:, 1])
            return basis.reshape(p.shape[0], -1)
        row, col = (edge_index[0], edge_index[1])
        basis = _basis(pseudo)
        messages = jnp.einsum('ek,ei,kio->eo', basis, x[row], weight)
        out = jnp.zeros((x.shape[0], weight.shape[2]), dtype=x.dtype).at[col].add(messages)
        degree = jnp.zeros((x.shape[0],), dtype=x.dtype).at[col].add(jnp.ones_like(col, dtype=x.dtype))
        out = out / jnp.maximum(degree, 1.0)[:, None]
        out = out + x @ root_w.T + root_b
        return out

    def _L1_gnn_ref(x, W, edge_type_weight, src, dst, edge_type):
        import jax, jax.numpy as jnp
        import numpy as np
        N_NODES = 6250
        N_EDGES = 200000
        D = 32
        NUM_BASES = 4
        NUM_RELATIONS = 8
        n_nodes = x.shape[0]
        num_bases = W.shape[0]
        out = jnp.zeros((n_nodes, W.shape[2]), dtype=x.dtype)
        x_src = x[src]
        for b in range(num_bases):
            m = x_src @ W[b]
            m = m * edge_type_weight[b][edge_type][:, None]
            out = out + jax.ops.segment_sum(m, dst, num_segments=n_nodes)
        return out
    edge_index = jnp.stack([src, dst])
    x = _layernorm(x + _L0_gnn_ref(x, edge_attr_2, L0_gnn_weight, L0_gnn_root_w, L0_gnn_root_b, edge_index), axis=-1)
    x = _layernorm(x + _L1_gnn_ref(x, L1_gnn_W, L1_gnn_edge_type_weight, src, dst, edge_type_8), axis=-1)
    return x

_drawn_inputs = setup_inputs


def setup_inputs(seed=0):
    import zlib

    import numpy as np

    out = dict(_drawn_inputs(seed))
    spreads = {}
    factors = {'L0_gnn_root_b': 5.814}
    for name, (base, spread) in spreads.items():
        noise = np.random.default_rng([zlib.crc32(name.encode()), seed]).standard_normal(out[name].shape)
        drawn = base * np.exp(spread * noise) if base else spread * noise
        out[name] = jnp.asarray(drawn.astype(out[name].dtype))
    for name, factor in factors.items():
        out[name] = (out[name] * factor).astype(out[name].dtype)
    return out
```

```python
import concourse.bass as bass
from concourse import mybir
from contextlib import ExitStack


def bass_spline_relational_gnn(nc, x, x_feat, src, dst, dst_run, attr, etype, spline_w, root_w, root_b, rel_w, rel_coef, out):
    fp32 = mybir.dt.float32
    i32 = mybir.dt.int32
    u32 = mybir.dt.uint32
    ALU = mybir.AluOpType
    ACT = mybir.ActivationFunctionType
    AX = mybir.AxisListType
    ds = bass.ds

    P = 128
    N, D = x.shape
    TILES = src.shape[1]
    C = 5
    S = 5
    CHUNKS = TILES // C
    STEPS = CHUNKS // S
    assert C * S * STEPS == TILES
    CE = C * P
    BLOCKS = (N + P - 1) // P
    FULL = N // P
    REST = N - FULL * P
    Q = 4
    BP = (BLOCKS + Q - 1) // Q * Q
    G3 = 3
    K = G3 * G3
    Z = K * D + 1
    R = rel_coef.shape[1]
    NB = rel_w.shape[0]
    RD = R * D
    EPS = 1e-5
    RP = 125
    RQ = CHUNKS // RP

    y_dram = nc.dram_tensor("y_rows", (BP * P * R, D), fp32, kind="Internal").ap()
    range_dram = nc.dram_tensor("chunk_ranges", (2, CHUNKS), i32, kind="Internal").ap()

    ctx = ExitStack()
    with ctx:
        def sb(name, shape, dt):
            return ctx.enter_context(nc.sbuf_tensor(name, shape, dt))

        def sem(name):
            return ctx.enter_context(nc.semaphore(name))

        zacc = sb("zacc", [P, BLOCKS * Z], fp32)
        src_sb = sb("src_sb", [P, TILES + C * S], i32)
        rel = sb("rel", [P, TILES], fp32)
        pseudo = sb("pseudo", [P, TILES * 2], fp32)
        h = sb("h", [P, BP * D], fp32)
        table = sb("table", [1, CHUNKS, 4], i32)
        idx = sb("idx", [P, S * C], u32)
        rows = sb("rows", [P, S * C, D], fp32)
        factor = sb("factor", [P, S, C, 2, G3], fp32)
        basis = sb("basis", [P, S, C, G3, G3], fp32)
        weighted = sb("weighted", [P, C, Z], fp32)
        onehot = sb("onehot", [P, C, P], fp32)
        rel_x = sb("rel_x", [P, C], fp32)
        iota = sb("iota", [P, P], fp32)
        block_base = sb("block_base", [P, BLOCKS], fp32)
        ident = sb("ident", [P, P], fp32)
        neg_grid = sb("neg_grid", [P, G3], fp32)
        eps_t = sb("eps_t", [P, 1], fp32)
        one_t = sb("one_t", [P, 1], fp32)
        wspline = sb("wspline", [G3 * D, G3, D], fp32)
        wroot = sb("wroot", [D + 1, D], fp32)
        wrel = sb("wrel", [P, NB, D], fp32)
        coef = sb("coef", [P, NB, R], fp32)
        rdeg = sb("rdeg", [P, BLOCKS], fp32)
        stat = sb("stat", [P, 4, BP], fp32)
        zscaled = sb("zscaled", [P, 2, K * D], fp32)
        zT = sb("zT", [G3 * D, 2, G3, P], fp32)

        xT = zacc[0:D + 1, 0:BLOCKS * P]
        at = BLOCKS * P
        runs = zacc[0:RP, at:at + RQ * CE].bitcast(i32).rearrange("r (q e) -> r q e", q=RQ)
        at += RQ * CE
        dst_i = zacc[:, at:at + TILES].bitcast(i32)
        at += TILES
        lo_all = zacc[:, at:at + CHUNKS].bitcast(i32)
        at += CHUNKS
        minmax = zacc[0:RP, at:at + 2 * RQ].bitcast(i32).rearrange("r (t q) -> r t q", t=2)
        at += 2 * RQ
        ranges = zacc[0:1, at:at + 2 * CHUNKS].bitcast(i32).rearrange("a (t c) -> a t c", t=2)
        at += 2 * CHUNKS
        extra_f = zacc[0:1, at:at + CHUNKS]
        at += CHUNKS
        scan_f = zacc[0:1, at:at + CHUNKS]
        assert at + CHUNKS <= BLOCKS * Z
        acc1 = zacc[:, 0:BP * D]
        tmp1 = zacc[:, BP * D:2 * BP * D]
        x1s = zacc[:, 2 * BP * D:2 * BP * D + 2 * P].rearrange("p (s n) -> p s n", s=2)
        o = 2 * BP * D + 2 * P
        x1T = zacc[:, o:o + 2 * P].rearrange("p (s n) -> p s n", s=2)
        o += 2 * P
        yout = zacc[:, o:o + 2 * Q * RD].rearrange("p (s q f) -> p s q f", s=2, q=Q)
        o += 2 * Q * RD
        wdiag = zacc[:, o:o + Q * RD]
        o += Q * RD
        weff, wtmp = (zacc[:, o + n * RD:o + (n + 1) * RD].rearrange("p (r d) -> p r d", d=D) for n in range(2))
        etype_i = pseudo[:, 0:TILES].bitcast(i32)
        hv = h[:, :].rearrange("p (b d) -> p b d", d=D)
        tv = tmp1.rearrange("p (b d) -> p b d", d=D)
        relv = rel[:, :].rearrange("p (c e) -> p c e", e=C)

        ps = ctx.enter_context(nc.psum_tensor("ps", [P, 8, 512], fp32))
        XB = S

        s_src = sem("s_src"); s_dst = sem("s_dst"); s_run = sem("s_run"); s_attr = sem("s_attr")
        s_x = sem("s_x"); s_xT = sem("s_xT"); s_w = sem("s_w"); s_rng = sem("s_rng")
        s_row = sem("s_row"); s_lo = sem("s_lo"); s_const = sem("s_const")
        s_mm_range = sem("s_mm_range"); s_table = sem("s_table"); s_pad = sem("s_pad"); s_ident = sem("s_ident")
        s_root = sem("s_root"); s_rooted = sem("s_rooted"); s_chain = sem("s_chain")
        s_tick = sem("s_tick")
        s_got = [sem(f"s_got{k}") for k in range(S)]
        s_staged = sem("s_staged"); s_abs = sem("s_abs"); s_factor = sem("s_factor")
        s_basis = sem("s_basis"); s_tile = sem("s_tile"); s_mm = sem("s_mm"); s_acc = sem("s_acc")
        s_relx = sem("s_relx"); s_ohx = sem("s_ohx"); s_psx = sem("s_psx"); s_accx = sem("s_accx")
        s_l0 = sem("s_l0"); s_rdeg = sem("s_rdeg"); s_zs = sem("s_zs"); s_zt = sem("s_zt")
        s_ztc = sem("s_ztc"); s_hp = sem("s_hp"); s_h = sem("s_h")
        s_var = sem("s_var"); s_sd = sem("s_sd"); s_ln = sem("s_ln")
        s_et = sem("s_et"); s_idx1 = sem("s_idx1"); s_wdiag = sem("s_wdiag"); s_x1s = sem("s_x1s"); s_x1p = sem("s_x1p")
        s_x1T = sem("s_x1T"); s_yp = sem("s_yp"); s_ya = sem("s_ya"); s_yd = sem("s_yd")
        s_y = [sem("s_y0"), sem("s_y1")]
        s_staged1 = sem("s_staged1")
        s_got1 = [sem(f"s_got1_{k}") for k in range(S)]
        s_tile1 = sem("s_tile1"); s_mm1 = sem("s_mm1"); s_acc1 = sem("s_acc1")
        s_relx1 = sem("s_relx1"); s_ohx1 = sem("s_ohx1"); s_psx1 = sem("s_psx1"); s_accx1 = sem("s_accx1")
        s_out = sem("s_out")

        TILE_CREDIT = S * C * 2
        MM_CREDIT = C
        MM1_CREDIT = S * C
        ACC_CREDIT = S - 1
        BASIS_CREDIT = S

        ROOT_GROUP = 14
        ROOT_GROUPS = BLOCKS // ROOT_GROUP
        assert ROOT_GROUPS * ROOT_GROUP == BLOCKS and ROOT_GROUPS <= 8

        YG = BP // Q

        block = ctx.enter_context(nc.Block())

        @block.sync
        def _(eng):
            eng.dma_start(runs, dst_run.rearrange("(r q) e -> r q e", q=RQ)).then_inc(s_run, 16)
            eng.dma_start(src_sb[:, 0:TILES], src).then_inc(s_src, 16)
            eng.dma_start(dst_i, dst).then_inc(s_dst, 16)
            eng.dma_start(xT[0:D, 0:N], x_feat).then_inc(s_xT, 16)
            eng.wait_ge(s_mm_range, 2)
            eng.dma_start(range_dram.rearrange("t (r q) -> r t q", q=RQ), minmax).then_inc(s_rng, 16)
            eng.wait_ge(s_rng, 16)
            eng.dma_start(ranges, range_dram.rearrange("(a t) c -> a t c", a=1)).then_inc(s_row, 16)
            eng.dma_start(lo_all, range_dram[0:1, :].to_broadcast((P, CHUNKS))).then_inc(s_lo, 16)
            eng.wait_ge(s_factor, CHUNKS)
            eng.dma_start(etype_i, etype).then_inc(s_et, 16)
            yv = y_dram.rearrange("(b p r) d -> p b (r d)", p=P, r=R)
            for g in range(YG):
                eng.wait_ge(s_ya, g + 1)
                eng.wait_ge(s_yd, g + 1)
                eng.dma_start(yv[:, Q * g:Q * (g + 1), :], yout[:, g % 2, :, :]).then_inc(s_y[g % 2], 16)
            eng.wait_ge(s_ln, 2)
            eng.dma_start(out[0:FULL * P, :].rearrange("(b p) d -> p b d", p=P), hv[:, 0:FULL, :]).then_inc(s_out, 16)
            eng.dma_start(out[FULL * P:N, :], hv[0:REST, FULL, :]).then_inc(s_out, 16)
            eng.wait_ge(s_out, 32)

        @block.gpsimd
        def _(eng):
            nc.gpsimd.iota(iota[:, :], [[1, P]], base=0, channel_multiplier=0,
                           allow_small_or_imprecise_dtypes=True).then_inc(s_const, 1)
            nc.gpsimd.iota(block_base[:, :], [[P, BLOCKS]], base=0, channel_multiplier=0,
                           allow_small_or_imprecise_dtypes=True).then_inc(s_const, 1)
            nc.gpsimd.memset(ident[:, :], 0.0).then_inc(s_ident, 1)
            eng.wait_ge(s_ident, 1)
            nc.gpsimd.affine_select(out=ident[:, :], in_=ident[:, :], compare_op=ALU.not_equal, fill=1.0,
                                    base=0, pattern=[[-1, P]], channel_multiplier=1).then_inc(s_const, 1)

            with eng.Fori(0, STEPS) as i:
                for k in range(S):
                    eng.wait_ge(s_tile, 2 * C * (S * i + k) + 2 * C)
                    eng.wait_ge(s_staged, S * i + k + 1)
                    eng.sem_inc(s_tick, 1)
                    for j in range(C):
                        t = k * C + j
                        nc.gpsimd.indirect_dma_start(
                            rows[:, t, :], None, x, bass.IndirectOffsetOnAxis(ap=idx[:, t:t + 1], axis=0)
                        ).then_inc(s_got[k], 16)

            eng.wait_ge(s_y[0], 16 * ((YG + 1) // 2))
            eng.wait_ge(s_y[1], 16 * (YG // 2))
            with eng.Fori(0, STEPS) as i:
                for k in range(S):
                    eng.wait_ge(s_mm1, C * (S * i + k) + 2 * C)
                    eng.wait_ge(s_staged1, S * i + k + 1)
                    eng.sem_inc(s_tick, 1)
                    for j in range(C):
                        t = k * C + j
                        nc.gpsimd.indirect_dma_start(
                            rows[:, t, :], None, y_dram, bass.IndirectOffsetOnAxis(ap=idx[:, t:t + 1], axis=0)
                        ).then_inc(s_got1[k], 16)

        @block.scalar
        def _(eng):
            eng.dma_start(pseudo[:, :], attr).then_inc(s_attr, 16)
            eng.dma_start(hv[:, 0:FULL, :], x[0:FULL * P, :].rearrange("(b p) d -> p b d", p=P)).then_inc(s_x, 16)
            eng.wait_ge(s_pad, 1)
            eng.dma_start(hv[0:REST, FULL, :], x[FULL * P:N, :]).then_inc(s_x, 16)
            eng.dma_start(wroot[0:D, :], root_w).then_inc(s_w, 16)
            eng.dma_start(wroot[D:D + 1, :], root_b).then_inc(s_w, 16)
            eng.dma_start(wspline[:, :, :], spline_w.rearrange("(a b) i o -> (b i) a o", a=G3)).then_inc(s_w, 16)
            for q in range(Q):
                eng.dma_start(wrel[q * D:(q + 1) * D, :, :], rel_w.rearrange("b i o -> i b o")).then_inc(s_w, 16)
            eng.dma_start(coef[:, :, :].rearrange("p b r -> p (b r)"),
                          rel_coef.rearrange("(a b) r -> a (b r)", a=1).to_broadcast((P, NB * R))).then_inc(s_w, 16)

            eng.wait_ge(s_src, 16)
            eng.wait_ge(s_pad, 2)
            nc.scalar.copy(idx[:, :], src_sb[:, 0:S * C]).then_inc(s_staged, S)
            eng.wait_ge(s_table, 2)

            with eng.Fori(0, STEPS) as i:
                for k in range(S):
                    c = S * i + k
                    eng.wait_ge(s_basis, c + 1)
                    eng.sem_inc(s_tick, 1)
                    for a in range(G3):
                        nc.scalar.activation(
                            factor[:, k, :, :, a],
                            pseudo[:, ds(2 * C * c, 2 * C)].rearrange("p (e d) -> p e d", d=2),
                            ACT.Abs, bias=neg_grid[:, a:a + 1], scale=1.0).then_inc(s_abs, 1)
                    eng.wait_ge(s_abs, G3 * c + G3)
                    nc.scalar.activation(factor[:, k, :, :, :].rearrange("p e d a -> p (e d a)"),
                                         factor[:, k, :, :, :].rearrange("p e d a -> p (e d a)"),
                                         ACT.Relu, bias=one_t[:, 0:1], scale=-(G3 - 1.0)).then_inc(s_factor, 1)
                    eng.wait_ge(s_got[k], 16 * C * (i + 1))
                    eng.sem_inc(s_tick, 1)
                    nc.scalar.copy(idx[:, k * C:(k + 1) * C], src_sb[:, ds(C * c + S * C, C)]).then_inc(s_staged, 1)

            eng.wait_ge(s_rdeg, 1)
            with eng.Fori(0, BLOCKS // 2) as i:
                for s in range(2):
                    b = 2 * i + s
                    eng.wait_ge(s_zt, b + 1)
                    eng.sem_inc(s_tick, 1)
                    nc.scalar.activation(zscaled[:, s, :], zacc[:, ds(Z * b, K * D)], ACT.Copy,
                                         scale=rdeg[:, ds(b, 1)]).then_inc(s_zs, 1)
            eng.wait_ge(s_var, 1)
            nc.scalar.activation(stat[:, 2, :], stat[:, 1, :], ACT.Sqrt, bias=eps_t[:, 0:1], scale=1.0 / D).then_inc(s_sd, 1)

            eng.wait_ge(s_ln, 1)
            for g in range(YG):
                s = g % 2
                eng.wait_ge(s_yp, g + 1)
                if g >= 2:
                    eng.wait_ge(s_y[s], 16 * (g // 2))
                nc.scalar.copy(yout[:, s, 0:2, :].rearrange("p a f -> p (a f)"), ps[:, 2 * s, :]).then_inc(s_ya, 1)

            eng.wait_ge(s_idx1, 2)
            eng.wait_ge(s_got[S - 1], 16 * C * STEPS)
            nc.scalar.copy(idx[:, :], src_sb[:, 0:S * C]).then_inc(s_staged1, S)
            with eng.Fori(0, STEPS) as i:
                for k in range(S):
                    eng.wait_ge(s_got1[k], 16 * C * (i + 1))
                    eng.sem_inc(s_tick, 1)
                    nc.scalar.copy(idx[:, k * C:(k + 1) * C],
                                   src_sb[:, ds(C * (S * i + k) + S * C, C)]).then_inc(s_staged1, 1)
            eng.wait_ge(s_var, 2)
            nc.scalar.activation(stat[:, 2, :], stat[:, 1, :], ACT.Sqrt, bias=eps_t[:, 0:1], scale=1.0 / D).then_inc(s_sd, 1)

        @block.vector
        def _(eng):
            chain = [0]

            def link(ins):
                chain[0] += 1
                ins.then_inc(s_chain, 1)
                eng.wait_ge(s_chain, chain[0])

            nc.vector.memset(h[:, FULL * D:BP * D], 0.0).then_inc(s_pad, 1)
            nc.vector.memset(src_sb[:, TILES:TILES + C * S], 0).then_inc(s_pad, 1)
            nc.vector.memset(xT[D:D + 1, :], 1.0)
            for a in range(G3):
                nc.vector.memset(neg_grid[:, a:a + 1], -float(a) / (G3 - 1))
            nc.vector.memset(eps_t[:, :], EPS)
            nc.vector.memset(one_t[:, :], 1.0)
            nc.vector.memset(xT[0:D, N:BLOCKS * P], 0.0)
            link(nc.vector.memset(weighted[:, :, K * D:Z], 1.0))

            eng.wait_ge(s_run, 16)
            nc.vector.tensor_reduce(minmax[:, 0, :], runs, AX.X, ALU.min)
            link(nc.vector.tensor_reduce(minmax[:, 1, :], runs, AX.X, ALU.max))
            nc.vector.tensor_scalar(minmax[:, :, :], minmax[:, :, :], 7, None, ALU.arith_shift_right).then_inc(s_mm_range, 2)
            eng.wait_ge(s_attr, 16)
            nc.vector.tensor_scalar(pseudo[:, :], pseudo[:, :], 0.0, 1.0, ALU.max, ALU.min).then_inc(s_table, 1)
            eng.wait_ge(s_dst, 16)
            link(nc.vector.tensor_copy(rel[:, :], dst_i))
            eng.wait_ge(s_row, 16)
            link(nc.vector.tensor_tensor(extra_f, ranges[:, 1, :], ranges[:, 0, :], ALU.subtract))
            link(nc.vector.tensor_tensor_scan(scan_f, extra_f, extra_f, 0.0, ALU.add, ALU.bypass))
            nc.vector.tensor_copy(table[:, :, 0], ranges[:, 0, :])
            nc.vector.tensor_copy(table[:, :, 1], extra_f)
            nc.vector.tensor_tensor(table[:, :, 2], scan_f, extra_f, ALU.subtract)
            nc.vector.memset(table[:, 0:1, 3], 0)
            nc.vector.tensor_copy(table[:, 1:CHUNKS, 3], ranges[:, 0, 0:CHUNKS - 1])
            eng.wait_ge(s_lo, 16)
            link(nc.vector.scalar_tensor_tensor(relv, lo_all.unsqueeze(2).to_broadcast((P, CHUNKS, C)), -float(P),
                                                relv, ALU.mult, ALU.add))
            eng.wait_ge(s_x, 32)
            for g in range(ROOT_GROUPS):
                eng.wait_ge(s_root, g + 1)
                w = ROOT_GROUP * D
                nc.vector.tensor_tensor(h[:, g * w:(g + 1) * w], h[:, g * w:(g + 1) * w], ps[:, g, 0:w],
                                        ALU.add).then_inc(s_rooted, 1)
            link(nc.vector.memset(zacc[:, :], 0.0))
            eng.wait_ge(s_const, 3)
            eng.sem_inc(s_table, 1)
            eng.sem_inc(s_tile, TILE_CREDIT)
            eng.sem_inc(s_acc, ACC_CREDIT)
            eng.sem_inc(s_basis, BASIS_CREDIT)
            eng.sem_inc(s_accx, 1)
            eng.sem_inc(s_acc1, ACC_CREDIT)
            eng.sem_inc(s_accx1, 1)

            with eng.Fori(0, STEPS) as i:
                for k in range(S):
                    c = S * i + k
                    extra = eng.value_load(table[0:1, ds(c, 1), 1], min_val=0, max_val=BLOCKS - 1)
                    before = eng.value_load(table[0:1, ds(c, 1), 2], min_val=0, max_val=BLOCKS * CHUNKS)
                    last_lo = eng.value_load(table[0:1, ds(c, 1), 3], min_val=0, max_val=BLOCKS - 1)
                    eng.wait_ge(s_factor, c + 1)
                    nc.vector.tensor_tensor(
                        basis[:, k, :, :, :],
                        factor[:, k, :, 0, :].unsqueeze(3).to_broadcast((P, C, G3, G3)),
                        factor[:, k, :, 1, :].unsqueeze(2).to_broadcast((P, C, G3, G3)),
                        ALU.mult).then_inc(s_basis, 1)
                    eng.wait_ge(s_got[k], 16 * C * (i + 1))
                    eng.wait_ge(s_basis, BASIS_CREDIT + c + 1)
                    for j in range(C):
                        eng.wait_ge(s_mm, C * c + j + 1)
                        nc.vector.tensor_scalar(onehot[:, j, :], iota[:, :], rel[:, ds(C * c + j, 1)], None,
                                                ALU.is_equal).then_inc(s_tile, 1)
                        nc.vector.tensor_tensor(
                            weighted[:, j, 0:K * D].rearrange("p (k d) -> p k d", d=D),
                            basis[:, k, j, :, :].rearrange("p a b -> p (a b)").unsqueeze(2).to_broadcast((P, K, D)),
                            rows[:, k * C + j, :].unsqueeze(1).to_broadcast((P, K, D)),
                            ALU.mult).then_inc(s_tile, 1)
                    eng.wait_ge(s_mm, MM_CREDIT + C * c)
                    eng.wait_ge(s_acc, ACC_CREDIT + c)
                    eng.wait_ge(s_accx, before + 1)
                    place = zacc[:, ds(last_lo * Z, Z)]
                    nc.vector.tensor_tensor(place, ps[:, (k - 1) % S, 0:Z], place, ALU.add).then_inc(s_acc, 1)
                    with eng.If(extra > 0):
                        first = eng.value_load(table[0:1, ds(c, 1), 0], min_val=0, max_val=BLOCKS - 1)
                        with eng.Fori(1, extra + 1) as e:
                            eng.wait_ge(s_mm, MM_CREDIT + C * (c + 1))
                            nc.vector.tensor_scalar(rel_x[:, :], rel[:, ds(C * c, C)], block_base[:, ds(e, 1)],
                                                    None, ALU.subtract).then_inc(s_relx, 1)
                            eng.wait_ge(s_relx, before + e)
                            for j in range(C):
                                nc.vector.tensor_scalar(onehot[:, j, :], iota[:, :], rel_x[:, j:j + 1], None,
                                                        ALU.is_equal).then_inc(s_ohx, 1)
                            eng.wait_ge(s_psx, before + e)
                            eng.wait_ge(s_acc, ACC_CREDIT + c + 1)
                            eng.wait_ge(s_accx, before + e)
                            place = zacc[:, ds((first + e).with_bounds(min_val=1, max_val=BLOCKS - 1) * Z, Z)]
                            nc.vector.tensor_tensor(place, ps[:, XB, 0:Z], place, ALU.add).then_inc(s_accx, 1)
            last = eng.value_load(table[0:1, CHUNKS - 1:CHUNKS, 0], min_val=0, max_val=BLOCKS - 1)
            last_n = eng.value_load(table[0:1, CHUNKS - 1:CHUNKS, 1], min_val=0, max_val=BLOCKS - 1)
            last_before = eng.value_load(table[0:1, CHUNKS - 1:CHUNKS, 2], min_val=0, max_val=BLOCKS * CHUNKS)
            eng.wait_ge(s_mm, MM_CREDIT + C * CHUNKS)
            eng.wait_ge(s_acc, ACC_CREDIT + CHUNKS)
            eng.wait_ge(s_accx, last_before + last_n + 1)
            place = zacc[:, ds(last * Z, Z)]
            nc.vector.tensor_tensor(place, ps[:, S - 1, 0:Z], place, ALU.add).then_inc(s_acc, 1)
            eng.wait_ge(s_acc, ACC_CREDIT + CHUNKS + 1)

            degree = zacc[:, :].rearrange("p (b z) -> p b z", z=Z)[:, :, K * D]
            link(nc.vector.tensor_scalar(rdeg[:, :], degree, 1.0, None, ALU.max))
            nc.vector.reciprocal(rdeg[:, :], rdeg[:, :]).then_inc(s_rdeg, 1)

            with eng.Fori(0, BLOCKS // 2) as i:
                for s in range(2):
                    b = 2 * i + s
                    eng.wait_ge(s_zt, b + 3)
                    eng.wait_ge(s_hp, b + 1)
                    nc.vector.tensor_copy(zT[:, s, :, :].rearrange("p g n -> p (g n)"),
                                          ps[0:G3 * D, s, 0:G3 * P]).then_inc(s_ztc, 1)
                    eng.wait_ge(s_hp, b + 3)
                    place = h[:, ds(b * D, D)]
                    nc.vector.tensor_tensor(place, ps[:, 2 + s, 0:D], place, ALU.add).then_inc(s_h, 1)
            eng.wait_ge(s_h, BLOCKS)

            def layernorm(final):
                mean, var, sd, rstd = (stat[:, n, :] for n in range(4))
                over = lambda v: v.unsqueeze(2).to_broadcast((P, BP, D))
                link(nc.vector.tensor_reduce(mean, hv, AX.X, ALU.add))
                link(nc.vector.scalar_tensor_tensor(hv, over(mean), -1.0 / D, hv, ALU.mult, ALU.add))
                link(nc.vector.tensor_tensor(tv, hv, hv, ALU.mult))
                nc.vector.tensor_reduce(var, tv, AX.X, ALU.add).then_inc(s_var, 1)
                eng.wait_ge(s_sd, final + 1)
                link(nc.vector.reciprocal(rstd, sd))
                nc.vector.tensor_tensor(hv, hv, over(rstd), ALU.mult).then_inc(s_ln, 1)

            layernorm(0)
            eng.wait_ge(s_ln, 1)
            link(nc.vector.memset(acc1, 0.0))

            eng.wait_ge(s_w, 16 * (4 + Q))
            for b in range(NB):
                dest = weff if b == 0 else wtmp
                link(nc.vector.tensor_tensor(dest[:, :, :], coef[:, b, :].unsqueeze(2).to_broadcast((P, R, D)),
                                             wrel[:, b, :].unsqueeze(1).to_broadcast((P, R, D)), ALU.mult))
                if b:
                    link(nc.vector.tensor_tensor(weff[:, :, :], weff[:, :, :], wtmp[:, :, :], ALU.add))
            link(nc.vector.memset(wdiag[:, :], 0.0))
            for q in range(Q):
                nc.vector.tensor_copy(wdiag[q * D:(q + 1) * D, q * RD:(q + 1) * RD],
                                      weff[q * D:(q + 1) * D, :, :].rearrange("p r d -> p (r d)")).then_inc(s_wdiag, 1)
            eng.wait_ge(s_et, 16)
            eng.wait_ge(s_staged, S + CHUNKS)
            nc.vector.scalar_tensor_tensor(src_sb[:, 0:TILES], src_sb[:, 0:TILES], float(R), etype_i,
                                           ALU.mult, ALU.add).then_inc(s_idx1, 2)

            for g in range(YG):
                s = g % 2
                if g >= 2:
                    eng.wait_ge(s_x1p, g - 1)
                nc.vector.tensor_copy(x1s[:, s, :], h[:, g * Q * D:(g + 1) * Q * D]).then_inc(s_x1s, 1)
                eng.wait_ge(s_x1p, g + 1)
                if g >= 2:
                    eng.wait_ge(s_yp, g - 1)
                nc.vector.tensor_copy(x1T[:, s, :], ps[:, 4 + s, 0:P]).then_inc(s_x1T, 1)
                eng.wait_ge(s_yp, g + 1)
                if g >= 2:
                    eng.wait_ge(s_y[s], 16 * (g // 2))
                nc.vector.tensor_copy(yout[:, s, 2:4, :].rearrange("p a f -> p (a f)"), ps[:, 2 * s + 1, :]).then_inc(s_yd, 1)

            with eng.Fori(0, STEPS) as i:
                for k in range(S):
                    c = S * i + k
                    extra = eng.value_load(table[0:1, ds(c, 1), 1], min_val=0, max_val=BLOCKS - 1)
                    before = eng.value_load(table[0:1, ds(c, 1), 2], min_val=0, max_val=BLOCKS * CHUNKS)
                    last_lo = eng.value_load(table[0:1, ds(c, 1), 3], min_val=0, max_val=BLOCKS - 1)
                    for j in range(C):
                        eng.wait_ge(s_mm1, MM1_CREDIT - C + C * c + j + 1)
                        nc.vector.tensor_scalar(onehot[:, j, :], iota[:, :], rel[:, ds(C * c + j, 1)], None,
                                                ALU.is_equal).then_inc(s_tile1, 1)
                    eng.wait_ge(s_mm1, MM1_CREDIT + C * c)
                    eng.wait_ge(s_acc1, ACC_CREDIT + c)
                    eng.wait_ge(s_accx1, before + 1)
                    place = acc1[:, ds(last_lo * D, D)]
                    nc.vector.tensor_tensor(place, ps[:, (k - 1) % S, 0:D], place, ALU.add).then_inc(s_acc1, 1)
                    with eng.If(extra > 0):
                        first = eng.value_load(table[0:1, ds(c, 1), 0], min_val=0, max_val=BLOCKS - 1)
                        with eng.Fori(1, extra + 1) as e:
                            eng.wait_ge(s_mm1, MM1_CREDIT + C * (c + 1))
                            nc.vector.tensor_scalar(rel_x[:, :], rel[:, ds(C * c, C)], block_base[:, ds(e, 1)],
                                                    None, ALU.subtract).then_inc(s_relx1, 1)
                            eng.wait_ge(s_relx1, before + e)
                            for j in range(C):
                                nc.vector.tensor_scalar(onehot[:, j, :], iota[:, :], rel_x[:, j:j + 1], None,
                                                        ALU.is_equal).then_inc(s_ohx1, 1)
                            eng.wait_ge(s_psx1, before + e)
                            eng.wait_ge(s_acc1, ACC_CREDIT + c + 1)
                            eng.wait_ge(s_accx1, before + e)
                            place = acc1[:, ds((first + e).with_bounds(min_val=1, max_val=BLOCKS - 1) * D, D)]
                            nc.vector.tensor_tensor(place, ps[:, XB, 0:D], place, ALU.add).then_inc(s_accx1, 1)
            eng.wait_ge(s_mm1, MM1_CREDIT + C * CHUNKS)
            eng.wait_ge(s_acc1, ACC_CREDIT + CHUNKS)
            eng.wait_ge(s_accx1, last_before + last_n + 1)
            place = acc1[:, ds(last * D, D)]
            link(nc.vector.tensor_tensor(place, ps[:, S - 1, 0:D], place, ALU.add))
            link(nc.vector.tensor_tensor(h[:, :], h[:, :], acc1, ALU.add))
            layernorm(1)

        @block.tensor
        def _(eng):
            eng.wait_ge(s_xT, 16)
            eng.wait_ge(s_w, 16 * (4 + Q))
            eng.wait_ge(s_chain, 1)
            for g in range(ROOT_GROUPS):
                for q in range(ROOT_GROUP):
                    b = g * ROOT_GROUP + q
                    mm = nc.tensor.matmul(ps[:, g, q * D:(q + 1) * D], xT[:, b * P:(b + 1) * P], wroot[:, :],
                                          start=True, stop=True)
                mm.then_inc(s_root, 1)
            eng.wait_ge(s_rooted, ROOT_GROUPS)
            eng.wait_ge(s_table, 2)
            nc.tensor.matmul(ps[:, S - 1, 0:Z], zacc[:, 0:P], zacc[:, 0:Z], start=True, stop=True).then_inc(s_mm, MM_CREDIT)

            with eng.Fori(0, STEPS) as i:
                for k in range(S):
                    c = S * i + k
                    extra = eng.value_load(table[0:1, ds(c, 1), 1], min_val=0, max_val=BLOCKS - 1)
                    before = eng.value_load(table[0:1, ds(c, 1), 2], min_val=0, max_val=BLOCKS * CHUNKS)
                    eng.wait_ge(s_acc, c + 1)
                    for j in range(C):
                        eng.wait_ge(s_tile, TILE_CREDIT + 2 * (C * c + j + 1))
                        nc.tensor.matmul(ps[:, k, 0:Z], onehot[:, j, :], weighted[:, j, :],
                                         start=(j == 0), stop=(j == C - 1)).then_inc(s_mm, 1)
                    with eng.If(extra > 0):
                        with eng.Fori(1, extra + 1) as e:
                            eng.wait_ge(s_accx, before + e)
                            for j in range(C):
                                eng.wait_ge(s_ohx, C * (before + e - 1) + j + 1)
                                mm = nc.tensor.matmul(ps[:, XB, 0:Z], onehot[:, j, :], weighted[:, j, :],
                                                      start=(j == 0), stop=(j == C - 1))
                            mm.then_inc(s_psx, 1)

            nc.tensor.matmul(ps[:, 6, 0:1], ident[:, :], ident[:, 0:1], start=True, stop=True).then_inc(s_zt, 2)
            nc.tensor.matmul(ps[:, 6, 0:1], ident[:, :], ident[:, 0:1], start=True, stop=True).then_inc(s_hp, 2)
            eng.wait_ge(s_acc, ACC_CREDIT + CHUNKS + 1)
            with eng.Fori(0, BLOCKS // 2) as i:
                for s in range(2):
                    b = 2 * i + s
                    eng.wait_ge(s_zs, b + 1)
                    for g in range(G3):
                        mm = nc.tensor.transpose(ps[0:G3 * D, s, g * P:(g + 1) * P],
                                                 zscaled[:, s, g * G3 * D:(g + 1) * G3 * D], ident[:, :])
                    mm.then_inc(s_zt, 1)
                    eng.wait_ge(s_ztc, b + 1)
                    for g in range(G3):
                        mm = nc.tensor.matmul(ps[:, 2 + s, 0:D], zT[:, s, g, :], wspline[:, g, :],
                                              start=(g == 0), stop=(g == G3 - 1))
                    mm.then_inc(s_hp, 1)

            eng.wait_ge(s_wdiag, Q)
            for g in range(YG):
                s = g % 2
                eng.wait_ge(s_x1s, g + 1)
                nc.tensor.transpose(ps[:, 4 + s, 0:P], x1s[:, s, :], ident[:, :]).then_inc(s_x1p, 1)
                eng.wait_ge(s_x1T, g + 1)
                if g >= 2:
                    eng.wait_ge(s_ya, g - 1)
                    eng.wait_ge(s_yd, g - 1)
                for q in range(2):
                    mm = nc.tensor.matmul(ps[:, 2 * s + q, :], x1T[:, s, :], wdiag[:, q * 2 * RD:(q + 1) * 2 * RD],
                                          start=True, stop=True)
                mm.then_inc(s_yp, 1)
            eng.wait_ge(s_ya, YG)
            eng.wait_ge(s_yd, YG)
            nc.tensor.matmul(ps[:, S - 1, 0:D], acc1[:, 0:P], acc1[:, 0:D], start=True, stop=True).then_inc(s_mm1, MM1_CREDIT)

            with eng.Fori(0, STEPS) as i:
                for k in range(S):
                    c = S * i + k
                    extra = eng.value_load(table[0:1, ds(c, 1), 1], min_val=0, max_val=BLOCKS - 1)
                    before = eng.value_load(table[0:1, ds(c, 1), 2], min_val=0, max_val=BLOCKS * CHUNKS)
                    eng.wait_ge(s_acc1, c + 1)
                    eng.wait_ge(s_got1[k], 16 * C * (i + 1))
                    for j in range(C):
                        eng.wait_ge(s_tile1, C * c + j + 1)
                        nc.tensor.matmul(ps[:, k, 0:D], onehot[:, j, :], rows[:, k * C + j, :],
                                         start=(j == 0), stop=(j == C - 1)).then_inc(s_mm1, 1)
                    with eng.If(extra > 0):
                        with eng.Fori(1, extra + 1) as e:
                            eng.wait_ge(s_accx1, before + e)
                            for j in range(C):
                                eng.wait_ge(s_ohx1, C * (before + e - 1) + j + 1)
                                mm = nc.tensor.matmul(ps[:, XB, 0:D], onehot[:, j, :], rows[:, k * C + j, :],
                                                      start=(j == 0), stop=(j == C - 1))
                            mm.then_inc(s_psx1, 1)


def kernel(x, src, dst, edge_attr_2, edge_type_8, L0_gnn_weight, L0_gnn_root_w, L0_gnn_root_b, L1_gnn_W, L1_gnn_edge_type_weight):
    import numpy as np
    import concourse.bacc as bacc
    from concourse.bass_utils import run_bass_kernel_spmd

    P, C = 128, 5
    x = np.ascontiguousarray(x)
    src, dst, etype = np.asarray(src), np.asarray(dst), np.asarray(edge_type_8)
    tiles = src.shape[0] // P
    by_tile = lambda a: np.ascontiguousarray(a.reshape(tiles, P).T)
    arrays = {
        "x": x,
        "x_feat": np.ascontiguousarray(x.T),
        "src": by_tile(src),
        "dst": by_tile(dst),
        "dst_run": np.ascontiguousarray(dst.reshape(tiles // C, C * P)),
        "attr": np.ascontiguousarray(np.asarray(edge_attr_2).reshape(tiles, P, 2).transpose(1, 0, 2).reshape(P, tiles * 2)),
        "etype": by_tile(etype),
        "spline_w": np.ascontiguousarray(L0_gnn_weight),
        "root_w": np.ascontiguousarray(np.asarray(L0_gnn_root_w).T),
        "root_b": np.ascontiguousarray(np.asarray(L0_gnn_root_b).reshape(1, -1)),
        "rel_w": np.ascontiguousarray(L1_gnn_W),
        "rel_coef": np.ascontiguousarray(L1_gnn_edge_type_weight),
    }
    nc = bacc.Bacc("TRN2", target_bir_lowering=False, num_devices=1)
    aps = [nc.dram_tensor(n, a.shape, mybir.dt.from_np(a.dtype), kind="ExternalInput").ap() for n, a in arrays.items()]
    out = nc.dram_tensor("out", x.shape, mybir.dt.float32, kind="ExternalOutput").ap()
    bass_spline_relational_gnn(nc, *aps, out)
    return run_bass_kernel_spmd(nc, [arrays], core_ids=[0]).results[0]["out"]
```
